# Optimizing a Trainium2 kernel written in Bass

```python
import numpy as np
import jax
import jax.numpy as jnp

def _softmax(x, axis=-1):
    return jax.nn.softmax(x, axis=axis)
def _gelu(x):
    return jax.nn.gelu(x, approximate=True)
def _silu(x):
    return jax.nn.silu(x)
def _sigmoid(x):
    return jax.nn.sigmoid(x)
def _layernorm(x, axis=-1, eps=1e-5):
    m = jnp.mean(x, axis=axis, keepdims=True)
    v = jnp.var(x, axis=axis, keepdims=True)
    return (x - m) / jnp.sqrt(v + eps)
def _scatter_add(tgt, idx, src, axis=0):
    return tgt.at[idx].add(src)
def _segment_sum(src, seg, n):
    return jax.ops.segment_sum(src, seg, n)

kernel_name = 'mk_conv_preact_d1_conv_nchw512_bbb6ce'

def setup_inputs(seed: int = 0):
    np.random.seed(seed)
    _w = jnp.asarray
    def _rec_inputs():
        import jax
        import jax.numpy as jnp
        _gk = jax.random.key(seed)
        x = -0.0003929 + 0.9999 * jax.random.normal(jax.random.fold_in(_gk, 1), (32, 512, 32, 32), jnp.float32)
        return x
    x = _rec_inputs()
    def _L0_conv_setup():
        import jax, jax.numpy as jnp
        import numpy as np
        key = jax.random.key(seed)
        k1, k2, k3 = jax.random.split(key, 3)
        b, c, h, w = (32, 512, 32, 32)
        x = jax.random.normal(k1, (b, c, h, w), dtype=jnp.float32)
        W = jax.random.normal(k2, (c, c), dtype=jnp.float32) * (1.0 / np.sqrt(c))
        bias = jax.random.normal(k3, (c,), dtype=jnp.float32) * 0.01
        return {'x': x, 'W': W, 'bias': bias}
    _L0_conv_all = _L0_conv_setup()
    _L0_conv_in = {k: v for k, v in _L0_conv_all.items() if k in ('W', 'bias', )}
    del _L0_conv_all

    return {
        "x": x,
        "L0_conv_W": _L0_conv_in["W"],
        "L0_conv_bias": _L0_conv_in["bias"],
    }

def reference(x, L0_conv_W, L0_conv_bias):
    import jax
    import jax.numpy as jnp
    def _L0_conv_ref(x, W, bias):
        import jax, jax.numpy as jnp
        import numpy as np
        b, c, h, w = x.shape
        n = h * w
        xf = x.reshape(b, c, n)
        y = jnp.einsum('bcn,oc->bon', xf, W) + bias[None, :, None]
        A = jax.nn.softmax(jnp.einsum('bcn,bdn->bcd', y, y), axis=-1)
        out = jnp.einsum('bcn,bcd->bnd', y, A)
        return out.reshape(b, c, h, w)

    def _gn(v, G=32, eps=1e-5):
        B_, C_, H_, W_ = v.shape
        g = v.reshape(B_, G, C_ // G, H_, W_)
        m = jnp.mean(g, axis=(2, 3, 4), keepdims=True)
        s = jnp.var(g, axis=(2, 3, 4), keepdims=True)
        return ((g - m) / jnp.sqrt(s + eps)).reshape(v.shape)

    def _ln_c(v, eps=1e-6):
        m = jnp.mean(v, axis=1, keepdims=True)
        s = jnp.var(v, axis=1, keepdims=True)
        return (v - m) / jnp.sqrt(s + eps)

    def _ln_t(v, eps=1e-5):
        m = jnp.mean(v, axis=-1, keepdims=True)
        s = jnp.var(v, axis=-1, keepdims=True)
        return (v - m) / jnp.sqrt(s + eps)

    def _to_tokens(v):
        B_, C_, H_, W_ = v.shape
        return v.reshape(B_, C_, H_ * W_).transpose(0, 2, 1)
    def _from_tokens(t, like):
        B_, C_, H_, W_ = like.shape
        return t.transpose(0, 2, 1).reshape(B_, C_, H_, W_)

    x = x + _L0_conv_ref(_gn(x), L0_conv_W, L0_conv_bias)
    return x


_drawn_inputs = setup_inputs


def setup_inputs(seed=0):
    import zlib

    import numpy as np

    out = dict(_drawn_inputs(seed))
    spreads = {}
    factors = {'L0_conv_bias': 8.0}
    for name, (base, spread) in spreads.items():
        noise = np.random.default_rng([zlib.crc32(name.encode()), seed]).standard_normal(out[name].shape)
        drawn = base * np.exp(spread * noise) if base else spread * noise
        out[name] = jnp.asarray(drawn.astype(out[name].dtype))
    for name, factor in factors.items():
        out[name] = (out[name] * factor).astype(out[name].dtype)
    return out
```

```python
from contextlib import ExitStack

import concourse.bass as bass
from concourse import mybir

ALU = mybir.AluOpType
ACT = mybir.ActivationFunctionType
AX = mybir.AxisListType
F32 = mybir.dt.float32
F16 = mybir.dt.float16
U32 = mybir.dt.uint32
I32 = mybir.dt.int32

P = 128
GROUPS = 32
GN_EPS = 1e-5
DMA = 16

XN_SCALE = 256.0
XN_BOUND = 128.0
FP16_TOP = 2.0 ** 14
PROB_SCALE = 2.0 ** 15
LEAST_BOUND = 2.0 ** -40
EXPONENT_BITS = 0x7F800000
RSQRT_SEED = float(0x5F3759DF)


class Batch:

    def __init__(self, pair, parity):
        self.pair, self.parity = pair, parity

    def plus(self, n):
        whole = self.parity + n
        return Batch(self.pair + whole // 2, whole % 2)

    def index(self):
        return self.pair * 2 + self.parity

    def count(self, per_batch, k):
        return self.pair * (2 * per_batch) + (self.parity * per_batch + k)


def bass_groupnorm_pointwise_conv_channel_attention_residual_kernel(
    nc: bass.Bass,
    x: bass.AP,
    W: bass.AP,
    bias: bass.AP,
    out: bass.AP,
):
    B, C, H, Wd = x.shape
    N = H * Wd
    CT = C // P
    NT = N // P
    HALF = N // 2
    GSIZE = C // GROUPS
    UNITS = 2 * CT
    SLOTS = 4
    BANK = 512
    ACCS = 4
    assert HALF == BANK == C and B % 2 == 0 and P % GSIZE == 0

    x_d = x.rearrange("b (t p) h w -> b p t (h w)", p=P)
    out_d = out.rearrange("b (t p) h w -> b p t (h w)", p=P)

    with ExitStack() as ctx:
        def sb(name, shape, dt):
            return ctx.enter_context(nc.sbuf_tensor(name, shape, dt))

        def sem(name):
            return ctx.enter_context(nc.semaphore(name))

        RUNS = 4

        x_sb = sb("x_sb", [P, SLOTS * CT * N], F32)
        xn = sb("xn", [P, 2, N], F32)
        xh = sb("xh", [P, CT, 2, HALF], F16)
        xl = sb("xl", [P, CT, 2, HALF], F16)
        y32 = sb("y32", [P, 2, HALF], F32)
        y16 = [sb(f"y16_{u}", [P, 2, CT, 2, HALF], F16) for u in range(2)]
        yT = sb("yT", [P, 2, 2, CT, C], F16)
        offd = sb("offd", [P, CT - 1, (CT - 1) * P], F32)
        E = sb("E", [P, CT, C], F32)
        Ah = sb("Ah", [P, CT, C], F16)
        Al = sb("Al", [P, CT, C], F16)
        w_sb = sb("w_sb", [P, CT, C], F32)
        wTh = sb("wTh", [P, CT, C], F16)
        wTl = sb("wTl", [P, CT, C], F16)
        ident = sb("ident", [P, P], F32)
        gmean = sb("gmean", [P, P], F32)
        b_sb = sb("b_sb", [P, CT], F32)
        b_abs = sb("b_abs", [P, CT], F32)
        w_l1 = sb("w_l1", [P, CT], F32)
        bounds = sb("bounds", [P, 2], F32)
        bounds_all = sb("bounds_all", [P, 2], F32)
        pow2 = sb("pow2", [P, 2], F32)
        scales = sb("scales", [P, 2], F32)
        unscales = sb("unscales", [P, 2], F32)
        y_scale = sb("y_scale", [P, 1], F32)
        y_bias = sb("y_bias", [P, CT], F32)
        kappa = sb("kappa", [P, 1], F32)
        neg_kappa = sb("neg_kappa", [P, 1], F32)
        out_scale = sb("out_scale", [P, 1], F32)
        bn = sb("bn", [P, CT, 2, 6], F32)
        sum_mean = sb("sum_mean", [P, CT], F32)
        gm = sb("gm", [P, CT], F32)
        dm = sb("dm", [P, CT, RUNS], F32)
        spread = sb("spread", [P, CT], F32)
        gv = sb("gv", [P, CT], F32)
        rs = [sb(f"rs{n}", [P, CT], F32) for n in range(4)]
        nt = sb("nt", [P, CT], F32)
        nu = sb("nu", [P, CT], F32)
        row_max = sb("row_max", [P, CT], F32)
        row_bias = sb("row_bias", [P, CT], F32)
        Z = sb("Z", [P, CT], F32)
        rz = sb("rz", [P, CT], F32)
        rz15 = sb("rz15", [P, CT], F32)

        runs = bn[:, :, :, :].rearrange("p t h (s k) -> p t (h s) k", k=3)
        run_mean, run_m2 = runs[:, :, :, 1], runs[:, :, :, 2]

        gram = [ctx.enter_context(nc.psum_tensor(f"gram{r}", [P, BANK], F32)) for r in range(CT)]
        acc = [ctx.enter_context(nc.psum_tensor(f"acc{r}", [P, BANK], F32)) for r in range(ACCS)]
        mix = gram[CT - 1]

        w_loaded = sem("w_loaded")
        b_loaded = sem("b_loaded")
        x_loaded = [sem(f"x_loaded{u}") for u in range(2)]
        stored = [sem(f"stored{u}") for u in range(2)]
        zeroed = sem("zeroed")
        consts_ready = sem("consts_ready")
        bounds_ready = sem("bounds_ready")
        bounds_spread = sem("bounds_spread")
        setup_step = sem("setup_step")
        scales_ready = sem("scales_ready")
        w_scaled = sem("w_scaled")
        w_turned = sem("w_turned")
        w_high = sem("w_high")
        w_low = sem("w_low")
        stats_step = sem("stats_step")
        means_ready = sem("means_ready")
        means_mixed = sem("means_mixed")
        mix_read = sem("mix_read")
        xn_ready = sem("xn_ready")
        xh_ready = sem("xh_ready")
        xl_ready = sem("xl_ready")
        y_summed = sem("y_summed")
        y32_ready = sem("y32_ready")
        yh_ready = sem("yh_ready")
        yl_ready = sem("yl_ready")
        turn_allowed = sem("turn_allowed")
        yT_ready = sem("yT_ready")
        row_summed = sem("row_summed")
        offd_ready = sem("offd_ready")
        row_mirrored = sem("row_mirrored")
        max_ready = sem("max_ready")
        row_bias_ready = sem("row_bias_ready")
        exp_ready = sem("exp_ready")
        recip_ready = sem("recip_ready")
        rz15_ready = sem("rz15_ready")
        ah_ready = sem("ah_ready")
        al_ready = sem("al_ready")
        out_summed = sem("out_summed")
        out_added = sem("out_added")

        NEWTON = 3
        STATS_STEPS = 2 * CT + 3 + 2 + 3 * NEWTON

        def need(eng, s, value):
            if not isinstance(value, int) or value > 0:
                eng.wait_ge(s, value)

        def x_slot(b, lo, size):
            if isinstance(b.pair, int):
                start = (b.index() % SLOTS) * CT * N + lo
                return x_sb[:, start:start + size]
            return x_sb[:, bass.ds((b.pair % 2) * (2 * CT * N) + (b.parity * CT * N + lo), size)]

        def batch_of(dram, b):
            if isinstance(b.pair, int):
                return dram[b.index()]
            return dram[bass.ds(b.index(), 1)].rearrange("b p t n -> (b p) t n")

        def steps(eng, step):
            step(Batch(-1, 0), False, False, True)
            step(Batch(-1, 1), False, True, True)
            step(Batch(0, 0), True, True, True)
            step(Batch(0, 1), True, True, True)
            with eng.Fori(1, B // 2 - 1) as pair:
                step(Batch(pair, 0), True, True, True)
                step(Batch(pair, 1), True, True, True)
            step(Batch(B // 2 - 1, 0), True, True, False)
            step(Batch(B // 2 - 1, 1), True, False, False)

        block = ctx.enter_context(nc.Block())

        @block.sync
        def _(sp):
            def load(b):
                sp.dma_start(x_slot(b, 0, CT * N).rearrange("p (t n) -> p t n", t=CT),
                             batch_of(x_d, b)).then_inc(x_loaded[b.parity], DMA)

            def store(b):
                for t in range(CT):
                    sp.wait_ge(out_added, b.count(UNITS, 2 * t + 2))
                    sp.dma_start(batch_of(out_d, b)[:, t, :],
                                 x_slot(b, t * N, N)).then_inc(stored[b.parity], DMA)

            def turn_y(b, u):
                h, m = u // CT, u % CT
                if u == 0:
                    need(sp, row_summed, b.count(CT, 0))
                    sp.sem_inc(turn_allowed, 1)
                sp.wait_ge(yl_ready, b.count(UNITS, u + 1))
                sp.sem_inc(turn_allowed, 1)
                sp.dma_start_transpose(
                    yT[:, h, :, :, m * P:(m + 1) * P].rearrange("p a j c -> p (a j) c"),
                    y16[b.parity][:, h, m, :, :].rearrange("p a q -> p (a q)")).then_inc(yT_ready, DMA)

            def refill(b):
                sp.wait_ge(stored[b.parity], (b.pair + 1) * (CT * DMA))
                sp.wait_ge(x_loaded[b.parity], (b.pair + 2) * DMA)
                load(b.plus(SLOTS))

            load(Batch(0, 0))
            sp.dma_start(w_sb[:, :, :], W.rearrange("(t p) k -> p t k", p=P)).then_inc(w_loaded, DMA)
            with nc.allow_non_contiguous_dma(reason="the bias, 4 bytes for each channel, once"):
                sp.dma_start(b_sb[:, :], bias.rearrange("(t p) -> p t", p=P)).then_inc(b_loaded, DMA)
            load(Batch(0, 1))
            for u in range(2):
                sp.wait_ge(x_loaded[u], DMA)
                load(Batch(1, u))
            def step(b, do_gram, do_y, do_load):
                if do_y:
                    for u in range(UNITS):
                        turn_y(b.plus(1), u)
                if do_gram:
                    store(b)
                if do_load:
                    refill(b)

            step(Batch(-1, 1), False, True, False)
            step(Batch(0, 0), True, True, True)
            step(Batch(0, 1), True, True, True)
            with sp.Fori(1, (B - SLOTS) // 2) as pair:
                step(Batch(pair, 0), True, True, True)
                step(Batch(pair, 1), True, True, True)
            for n in range(B - SLOTS, B):
                step(Batch(n // 2, n % 2), True, n + 1 < B, False)
            for u in range(2):
                sp.wait_ge(stored[u], B // 2 * CT * DMA)

        @block.gpsimd
        def _(pool):
            nc.gpsimd.memset(ident[:, :], 0.0).then_inc(zeroed, 1)
            nc.gpsimd.memset(gmean[:, :], 1.0 / GSIZE).then_inc(zeroed, 1)
            pool.wait_ge(zeroed, 2)
            nc.gpsimd.affine_select(out=ident[:, :], in_=ident[:, :], compare_op=ALU.not_equal, fill=1.0,
                                    base=0, pattern=[[-1, P]], channel_multiplier=1).then_inc(zeroed, 1)
            blocks = gmean[:, :].rearrange("p (g j) -> p g j", j=GSIZE)
            nc.gpsimd.affine_select(out=blocks, in_=blocks, compare_op=ALU.is_ge, fill=0.0, base=0,
                                    pattern=[[-GSIZE, P // GSIZE], [0, GSIZE]],
                                    channel_multiplier=1).then_inc(zeroed, 1)
            pool.wait_ge(zeroed, 4)
            nc.gpsimd.affine_select(out=blocks, in_=blocks, compare_op=ALU.is_ge, fill=0.0, base=GSIZE - 1,
                                    pattern=[[GSIZE, P // GSIZE], [0, GSIZE]],
                                    channel_multiplier=-1).then_inc(consts_ready, 1)
            pool.wait_ge(bounds_ready, 1)
            nc.gpsimd.partition_all_reduce(bounds_all[:, :], bounds[:, :], P,
                                           bass.bass_isa.ReduceOp.max).then_inc(bounds_spread, 1)

        @block.tensor
        def _(pe):
            pe.wait_ge(consts_ready, 1)
            pe.wait_ge(w_scaled, 1)
            for k in range(CT):
                for m in range(CT):
                    mm = nc.tensor.transpose(gram[k][:, m * P:(m + 1) * P],
                                             w_sb[:, m, k * P:(k + 1) * P], ident[:, :])
                mm.then_inc(w_turned, 1)

            def gram_row(b, r, y_follows):
                bank = gram[r][:, r * P:C]
                rows = slice(r * P, (r + 1) * P)
                if r == CT - 1 and y_follows:
                    pe.wait_ge(mix_read, b.plus(1).count(2, 2))
                need(pe, exp_ready, b.count(CT, 0))
                if r == 0:
                    pe.wait_ge(yT_ready, b.count(UNITS * DMA, UNITS * DMA))
                for j in range(NT):
                    h, jt = j // CT, j % CT
                    for a, c in ((0, 0), (0, 1), (1, 0)):
                        mm = nc.tensor.matmul(bank, yT[:, h, a, jt, rows], yT[:, h, c, jt, r * P:C],
                                              start=(j == 0 and a == c), stop=(j == NT - 1 and a == 1))
                mm.then_inc(row_summed, 1)

            def mirror_row(b, r):
                pe.wait_ge(offd_ready, b.count(CT - 1, min(r + 1, CT - 1)))
                for c in range(r):
                    mm = nc.tensor.transpose(gram[r][:, c * P:(c + 1) * P],
                                             offd[:, c, (r - c - 1) * P:(r - c) * P], ident[:, :])
                mm.then_inc(row_mirrored, 1)

            def y_unit(b, u):
                h, m = u // CT, u % CT
                if u < ACCS:
                    need(pe, out_added, b.plus(-1).count(UNITS, 0))
                else:
                    pe.wait_ge(yh_ready, b.count(UNITS, u - ACCS + 1))
                for k in range(CT):
                    if u == 0:
                        pe.wait_ge(xh_ready, b.count(CT, k + 1))
                        pe.wait_ge(xl_ready, b.count(CT, k + 1))
                    cols = slice(m * P, (m + 1) * P)
                    for wt, xt in ((wTh, xh), (wTh, xl), (wTl, xh)):
                        mm = nc.tensor.matmul(acc[u % ACCS][:, :], wt[:, k, cols], xt[:, k, h, :],
                                              start=(k == 0 and wt is wTh and xt is xh),
                                              stop=(k == CT - 1 and wt is wTl))
                mm.then_inc(y_summed, 1)

            def out_unit(b, u, y_follows):
                t, h = u // 2, u % 2
                if u >= ACCS:
                    pe.wait_ge(out_added, b.count(UNITS, u - ACCS + 1))
                elif y_follows:
                    pe.wait_ge(yh_ready, b.plus(1).count(UNITS, UNITS - ACCS + u + 1))
                for k in range(CT):
                    if u == 0:
                        pe.wait_ge(ah_ready, b.count(CT, k + 1))
                        pe.wait_ge(al_ready, b.count(CT, k + 1))
                    rows = slice(t * P, (t + 1) * P)
                    for a, at in ((0, Ah), (0, Al), (1, Ah)):
                        mm = nc.tensor.matmul(acc[u % ACCS][:, :], y16[b.parity][:, h, k, a, rows], at[:, k, :],
                                              start=(k == 0 and a == 0 and at is Ah),
                                              stop=(k == CT - 1 and a == 1))
                mm.then_inc(out_summed, 1)

            def mix_means(b, k):
                pe.wait_ge(means_ready, b.count(2, k + 1))
                if k == 0:
                    need(pe, exp_ready, b.plus(-1).count(CT, 0))
                rhs = sum_mean[:, :] if k == 0 else spread[:, :]
                nc.tensor.matmul(mix[:, k * CT:(k + 1) * CT], gmean[:, :], rhs,
                                 start=True, stop=True).then_inc(means_mixed, 1)

            def step(b, do_gram, do_y, do_norm):
                nxt, norm = b.plus(1), b.plus(2)
                if do_gram:
                    gram_row(b, 0, do_y)
                    gram_row(b, 1, do_y)
                    gram_row(b, 2, do_y)
                    mirror_row(b, 1)
                    gram_row(b, 3, do_y)
                for u in range(UNITS):
                    if do_y:
                        y_unit(nxt, u)
                    if u == 0 and do_gram:
                        mirror_row(b, 2)
                        mirror_row(b, 3)
                for u in range(UNITS):
                    if do_gram:
                        out_unit(b, u, do_y)
                    if do_norm and u == 1:
                        mix_means(norm, 0)
                    if do_norm and u == 3:
                        mix_means(norm, 1)

            pe.wait_ge(w_low, CT)
            pe.wait_ge(w_high, CT)
            steps(pe, step)

        @block.scalar
        def _(act):
            for k in range(CT):
                act.wait_ge(w_turned, k + 1)
                nc.scalar.activation(wTh[:, k, :], gram[k][:, :], ACT.Copy).then_inc(w_high, 1)
            act.wait_ge(scales_ready, 1)

            def exp_row(b, r):
                act.wait_ge(row_bias_ready, b.count(CT, r + 1))
                need(act, al_ready, b.count(CT, 0))
                nc.scalar.activation(E[:, r, :], gram[r][:, :], ACT.Exp, bias=row_bias[:, r:r + 1],
                                     scale=kappa[:, 0:1], accum_out=Z[:, r:r + 1]).then_inc(exp_ready, 1)

            def prob_high(b, r):
                act.wait_ge(rz15_ready, b.count(CT, r + 1))
                need(act, out_summed, b.count(UNITS, 0))
                nc.scalar.activation(Ah[:, r, :], E[:, r, :], ACT.Copy,
                                     scale=rz15[:, r:r + 1]).then_inc(ah_ready, 1)

            def y_high(b, u):
                h, m = u // CT, u % CT
                act.wait_ge(y_summed, b.count(UNITS, u + 1))
                need(act, yl_ready, b.count(UNITS, u - 1))
                need(act, out_summed, b.plus(-1).count(UNITS, 0))
                nc.scalar.activation(y32[:, u % 2, :], acc[u % ACCS][:, :], ACT.Identity,
                                     bias=y_bias[:, m:m + 1], scale=y_scale[:, 0:1]).then_inc(y32_ready, 1)
                nc.scalar.activation(y16[b.parity][:, h, m, 0, :], acc[u % ACCS][:, :], ACT.Identity,
                                     bias=y_bias[:, m:m + 1], scale=y_scale[:, 0:1]).then_inc(yh_ready, 1)

            def x_high(b, t):
                act.wait_ge(xn_ready, b.count(CT, t + 1))
                need(act, y_summed, b.count(UNITS, 0))
                nc.scalar.activation(xh[:, t, :, :], xn[:, t % 2, :].rearrange("p (q h) -> p h q", h=2),
                                     ACT.Copy).then_inc(xh_ready, 1)

            def step(b, do_gram, do_y, do_norm):
                nxt, norm = b.plus(1), b.plus(2)
                if do_gram:
                    exp_row(b, 0)
                    exp_row(b, 1)
                    prob_high(b, 0)
                for u in range(UNITS):
                    if do_y:
                        y_high(nxt, u)
                    if do_gram:
                        if u == 0:
                            exp_row(b, 2)
                            prob_high(b, 1)
                            exp_row(b, 3)
                        if u in (1, 2):
                            prob_high(b, u + 1)
                if do_norm:
                    for t in range(CT):
                        x_high(norm, t)

            steps(act, step)

        @block.vector
        def _(dve):
            v = nc.vector

            count = [0]

            def chain(ins):
                count[0] += 1
                ins.then_inc(setup_step, 1)
                dve.wait_ge(setup_step, count[0])

            dve.wait_ge(w_loaded, DMA)
            v.tensor_reduce(w_l1[:, :], w_sb[:, :, :], AX.X, ALU.add, apply_absolute_value=True)
            v.tensor_reduce(bounds[:, 0:1], w_sb[:, :, :], AX.XY, ALU.max, apply_absolute_value=True)
            dve.wait_ge(b_loaded, DMA)
            chain(v.tensor_reduce(b_abs[:, :], b_sb[:, :].rearrange("p (t o) -> p t o", o=1), AX.X, ALU.max,
                                  apply_absolute_value=True))
            chain(v.scalar_tensor_tensor(w_l1[:, :], w_l1[:, :], XN_BOUND, b_abs[:, :], ALU.mult, ALU.add))
            v.tensor_reduce(bounds[:, 1:2], w_l1[:, :], AX.X, ALU.max).then_inc(bounds_ready, 1)
            dve.wait_ge(bounds_spread, 1)
            chain(v.tensor_scalar(bounds_all[:, :], bounds_all[:, :], LEAST_BOUND, None, ALU.max))
            chain(v.tensor_scalar(pow2[:, :].bitcast(U32), bounds_all[:, :].bitcast(U32), EXPONENT_BITS, None,
                                  ALU.bitwise_and))
            chain(v.reciprocal(scales[:, :], pow2[:, :]))
            v.tensor_scalar(unscales[:, :], pow2[:, :], 1.0 / FP16_TOP, None, ALU.mult)
            chain(v.tensor_scalar(scales[:, :], scales[:, :], FP16_TOP, None, ALU.mult))
            v.tensor_scalar(w_sb[:, :, :], w_sb[:, :, :], scales[:, 0:1], None, ALU.mult).then_inc(w_scaled, 1)
            v.tensor_scalar(y_bias[:, :], b_sb[:, :], scales[:, 1:2], None, ALU.mult)
            v.tensor_scalar(out_scale[:, :], unscales[:, 1:2], 1.0 / PROB_SCALE, None, ALU.mult)
            chain(v.tensor_scalar(kappa[:, :], unscales[:, 1:2], unscales[:, 1:2], None, ALU.mult))
            v.tensor_scalar(neg_kappa[:, :], kappa[:, :], -1.0, None, ALU.mult)
            v.tensor_scalar(y_scale[:, :], scales[:, 1:2], unscales[:, 0:1], 1.0 / XN_SCALE,
                            ALU.mult, ALU.mult).then_inc(scales_ready, 1)
            dve.wait_ge(scales_ready, 1)
            for k in range(CT):
                dve.wait_ge(w_high, k + 1)
                v.tensor_tensor(wTl[:, k, :], gram[k][:, :], wTh[:, k, :], ALU.subtract).then_inc(w_low, 1)

            def channel_stats(b, piece):
                t, h = piece // 2, piece % 2
                if piece == 0:
                    dve.wait_ge(x_loaded[b.parity], (b.pair + 1) * DMA)
                v.bn_stats(bn[:, t, h, :], x_slot(b, t * N + h * HALF, HALF)).then_inc(stats_step, 1)

            def channel_means(b):
                dve.wait_ge(stats_step, b.count(STATS_STEPS, 2 * CT))
                v.tensor_reduce(sum_mean[:, :], run_mean, AX.X, ALU.add).then_inc(means_ready, 1)

            def group_mean(b):
                dve.wait_ge(means_mixed, b.count(2, 1))
                v.tensor_scalar(gm[:, :], mix[:, 0:CT], 1.0 / RUNS, None, ALU.mult).then_inc(mix_read, 1)
                dve.wait_ge(mix_read, b.count(2, 1))
                v.tensor_tensor(dm[:, :, :], run_mean, gm[:, :].unsqueeze(2).broadcast_to([P, CT, RUNS]),
                                ALU.subtract).then_inc(stats_step, 1)
                dve.wait_ge(stats_step, b.count(STATS_STEPS, 2 * CT + 1))
                v.tensor_tensor(dm[:, :, :], dm[:, :, :], dm[:, :, :], ALU.mult).then_inc(stats_step, 1)
                dve.wait_ge(stats_step, b.count(STATS_STEPS, 2 * CT + 2))
                v.scalar_tensor_tensor(dm[:, :, :], run_m2, RUNS / N, dm[:, :, :],
                                       ALU.mult, ALU.add).then_inc(stats_step, 1)
                dve.wait_ge(stats_step, b.count(STATS_STEPS, 2 * CT + 3))
                v.tensor_reduce(spread[:, :], dm[:, :, :], AX.X, ALU.add).then_inc(means_ready, 1)

            def group_rsqrt(b):
                k = 2 * CT + 3
                dve.wait_ge(means_mixed, b.count(2, 2))
                v.tensor_scalar(gv[:, :], mix[:, CT:2 * CT], RUNS * GN_EPS, XN_SCALE ** -2 / RUNS,
                                ALU.add, ALU.mult).then_inc(mix_read, 1)
                dve.wait_ge(mix_read, b.count(2, 2))
                v.tensor_scalar(nt[:, :].bitcast(I32), gv[:, :].bitcast(I32), 1, None,
                                ALU.arith_shift_right).then_inc(stats_step, 1)
                k += 1
                dve.wait_ge(stats_step, b.count(STATS_STEPS, k))
                v.tensor_scalar(rs[0][:, :].bitcast(I32), nt[:, :].bitcast(I32), -1.0, RSQRT_SEED,
                                ALU.mult, ALU.add).then_inc(stats_step, 1)
                k += 1
                for n in range(NEWTON):
                    dve.wait_ge(stats_step, b.count(STATS_STEPS, k))
                    v.scalar_tensor_tensor(nt[:, :], rs[n][:, :], -0.5, rs[n][:, :],
                                           ALU.mult, ALU.mult).then_inc(stats_step, 1)
                    dve.wait_ge(stats_step, b.count(STATS_STEPS, k + 1))
                    v.tensor_tensor(nu[:, :], nt[:, :], gv[:, :], ALU.mult).then_inc(stats_step, 1)
                    dve.wait_ge(stats_step, b.count(STATS_STEPS, k + 2))
                    v.scalar_tensor_tensor(rs[n + 1][:, :], nu[:, :], 1.5, rs[n][:, :],
                                           ALU.add, ALU.mult).then_inc(stats_step, 1)
                    k += 3
                assert k == STATS_STEPS

            def x_normalise(b, t):
                if t == 0:
                    dve.wait_ge(stats_step, b.count(STATS_STEPS, STATS_STEPS))
                need(dve, xh_ready, b.count(CT, t - 1))
                need(dve, xl_ready, b.count(CT, t - 1))
                v.tensor_scalar(xn[:, t % 2, :], x_slot(b, t * N, N), gm[:, t:t + 1],
                                rs[NEWTON][:, t:t + 1], ALU.subtract, ALU.mult).then_inc(xn_ready, 1)

            def x_low(b, t):
                dve.wait_ge(xh_ready, b.count(CT, t + 1))
                v.tensor_tensor(xl[:, t, :, :], xn[:, t % 2, :].rearrange("p (q h) -> p h q", h=2),
                                xh[:, t, :, :], ALU.subtract).then_inc(xl_ready, 1)

            def keep_offdiagonal(b, r):
                dve.wait_ge(row_summed, b.count(CT, r + 1))
                need(dve, row_mirrored, b.count(CT - 1, 0))
                v.tensor_copy(offd[:, r, 0:(CT - 1 - r) * P], gram[r][:, (r + 1) * P:C]).then_inc(offd_ready, 1)

            def row_maximum(b, r):
                if r > 0:
                    dve.wait_ge(row_mirrored, b.count(CT - 1, r))
                need(dve, exp_ready, b.count(CT, 0))
                v.tensor_reduce(row_max[:, r:r + 1], gram[r][:, :], AX.X, ALU.max).then_inc(max_ready, 1)
                dve.wait_ge(max_ready, b.count(CT, r + 1))
                v.tensor_scalar(row_bias[:, r:r + 1], row_max[:, r:r + 1], neg_kappa[:, 0:1], None,
                                ALU.mult).then_inc(row_bias_ready, 1)

            def row_reciprocal(b, r):
                dve.wait_ge(exp_ready, b.count(CT, r + 1))
                v.reciprocal(rz[:, r:r + 1], Z[:, r:r + 1]).then_inc(recip_ready, 1)
                dve.wait_ge(recip_ready, b.count(CT, r + 1))
                v.tensor_scalar(rz15[:, r:r + 1], rz[:, r:r + 1], PROB_SCALE, None,
                                ALU.mult).then_inc(rz15_ready, 1)

            def prob_low(b, r):
                dve.wait_ge(ah_ready, b.count(CT, r + 1))
                v.scalar_tensor_tensor(Al[:, r, :], E[:, r, :], rz15[:, r:r + 1], Ah[:, r, :],
                                       ALU.mult, ALU.subtract).then_inc(al_ready, 1)

            def y_low(b, u):
                h, m = u // CT, u % CT
                dve.wait_ge(yh_ready, b.count(UNITS, u + 1))
                v.tensor_tensor(y16[b.parity][:, h, m, 1, :], y32[:, u % 2, :], y16[b.parity][:, h, m, 0, :],
                                ALU.subtract).then_inc(yl_ready, 1)

            def add_out(b, u):
                t, h = u // 2, u % 2
                dve.wait_ge(out_summed, b.count(UNITS, u + 1))
                x_part = x_slot(b, t * N + h * HALF, HALF)
                v.scalar_tensor_tensor(x_part, acc[u % ACCS][:, :], out_scale[:, 0:1], x_part,
                                       ALU.mult, ALU.add).then_inc(out_added, 1)

            def step(b, do_gram, do_y, do_norm):
                nxt, norm = b.plus(1), b.plus(2)

                def stats(*pieces):
                    if do_norm:
                        for piece in pieces:
                            channel_stats(norm, piece)

                stats(0, 1)
                if do_gram:
                    keep_offdiagonal(b, 0)
                    row_maximum(b, 0)
                stats(2, 3)
                if do_gram:
                    keep_offdiagonal(b, 1)
                    row_reciprocal(b, 0)
                stats(4)
                if do_gram:
                    keep_offdiagonal(b, 2)
                    row_maximum(b, 1)
                    prob_low(b, 0)
                stats(5, 6, 7)
                if do_gram:
                    row_reciprocal(b, 1)
                    row_maximum(b, 2)
                    row_maximum(b, 3)
                    prob_low(b, 1)
                if do_norm:
                    channel_means(norm)
                for u in range(UNITS):
                    if do_gram and u in (1, 2):
                        row_reciprocal(b, u + 1)
                    if do_y:
                        y_low(nxt, u)
                    if do_gram and u in (2, 3):
                        prob_low(b, u)
                for u in range(UNITS):
                    if do_gram:
                        add_out(b, u)
                    if do_norm:
                        if u == 2:
                            group_mean(norm)
                        if u == 4:
                            group_rsqrt(norm)
                            x_normalise(norm, 0)
                            x_normalise(norm, 1)
                        if u == 5:
                            x_low(norm, 0)
                            x_normalise(norm, 2)
                        if u == 6:
                            x_low(norm, 1)
                            x_normalise(norm, 3)
                        if u == 7:
                            x_low(norm, 2)
                            x_low(norm, 3)

            steps(dve, step)


_INS = ['x', 'L0_conv_W', 'L0_conv_bias']
_OUTS = [((32, 512, 32, 32), 'float32')]


def kernel(**inputs):
    import numpy as _np
    import concourse.bacc as _bacc
    from concourse import mybir as _mybir
    from concourse.bass_utils import run_bass_kernel_spmd as _run

    nc = _bacc.Bacc("TRN2", target_bir_lowering=False, num_devices=1)
    arrays, args = {}, []
    for name in _INS:
        a = _np.ascontiguousarray(inputs[name])
        arrays[f"in_{name}_dram"] = a
        args.append(nc.dram_tensor(f"in_{name}_dram", a.shape, _mybir.dt.from_np(a.dtype), kind="ExternalInput").ap())
    for i, (shape, dtype) in enumerate(_OUTS):
        dt = _mybir.dt.from_np(_np.dtype(dtype))
        args.append(nc.dram_tensor(f"out_{i}_dram", shape, dt, kind="ExternalOutput").ap())
    bass_groupnorm_pointwise_conv_channel_attention_residual_kernel(nc, *args)
    r = _run(nc, [arrays], core_ids=[0])
    got = tuple(r.results[0][f"out_{i}_dram"] for i in range(len(_OUTS)))
    return got[0]
```

```python
from contextlib import ExitStack

import concourse.bass as bass
from concourse import mybir

ALU = mybir.AluOpType
ACT = mybir.ActivationFunctionType
AX = mybir.AxisListType
F32 = mybir.dt.float32
F16 = mybir.dt.float16
U32 = mybir.dt.uint32
I32 = mybir.dt.int32

P = 128
GROUPS = 32
GN_EPS = 1e-5
DMA = 16

XN_SCALE = 256.0
XN_BOUND = 128.0
FP16_TOP = 2.0 ** 14
PROB_SCALE = 2.0 ** 15
LEAST_BOUND = 2.0 ** -40
EXPONENT_BITS = 0x7F800000
RSQRT_SEED = float(0x5F3759DF)


class Batch:

    def __init__(self, pair, parity):
        self.pair, self.parity = pair, parity

    def plus(self, n):
        whole = self.parity + n
        return Batch(self.pair + whole // 2, whole % 2)

    def index(self):
        return self.pair * 2 + self.parity

    def count(self, per_batch, k):
        return self.pair * (2 * per_batch) + (self.parity * per_batch + k)


def bass_groupnorm_pointwise_conv_channel_attention_residual_kernel(
    nc: bass.Bass,
    x: bass.AP,
    W: bass.AP,
    bias: bass.AP,
    out: bass.AP,
):
    B, C, H, Wd = x.shape
    N = H * Wd
    CT = C // P
    NT = N // P
    HALF = N // 2
    GSIZE = C // GROUPS
    UNITS = 2 * CT
    SLOTS = 4
    BANK = 512
    ACCS = 4
    assert HALF == BANK == C and B % 2 == 0 and P % GSIZE == 0

    x_d = x.rearrange("b (t p) h w -> b p t (h w)", p=P)
    out_d = out.rearrange("b (t p) h w -> b p t (h w)", p=P)

    with ExitStack() as ctx:
        def sb(name, shape, dt):
            return ctx.enter_context(nc.sbuf_tensor(name, shape, dt))

        def sem(name):
            return ctx.enter_context(nc.semaphore(name))

        RUNS = 4

        x_sb = sb("x_sb", [P, SLOTS * CT * N], F32)
        xn = sb("xn", [P, 2, N], F32)
        xh = sb("xh", [P, CT, 2, HALF], F16)
        xl = sb("xl", [P, CT, 2, HALF], F16)
        y32 = sb("y32", [P, 2, HALF], F32)
        y16 = [sb(f"y16_{u}", [P, 2, CT, 2, HALF], F16) for u in range(2)]
        yT = sb("yT", [P, 2, 2, CT, C], F16)
        yTs = sb("yTs", [P, 2, CT, C], F16)
        upper = sb("upper", [P, CT, C], F32)
        E = sb("E", [P, CT, C], F32)
        Ah = sb("Ah", [P, CT, C], F16)
        Al = sb("Al", [P, CT, C], F16)
        w_sb = sb("w_sb", [P, CT, C], F32)
        wTh = sb("wTh", [P, CT, C], F16)
        wTl = sb("wTl", [P, CT, C], F16)
        ident = sb("ident", [P, P], F32)
        gmean = sb("gmean", [P, P], F32)
        b_sb = sb("b_sb", [P, CT], F32)
        b_abs = sb("b_abs", [P, CT], F32)
        w_l1 = sb("w_l1", [P, CT], F32)
        y_l1 = sb("y_l1", [P, CT], F32)
        bounds = sb("bounds", [P, 2], F32)
        bounds_all = sb("bounds_all", [P, 2], F32)
        pow2 = sb("pow2", [P, 2], F32)
        scales = sb("scales", [P, 2], F32)
        unscales = sb("unscales", [P, 2], F32)
        y_scale = sb("y_scale", [P, 1], F32)
        y_bias = sb("y_bias", [P, CT], F32)
        kappa = sb("kappa", [P, 1], F32)
        neg_kappa = sb("neg_kappa", [P, 1], F32)
        out_scale = sb("out_scale", [P, 1], F32)
        bn = sb("bn", [P, CT, 2, 6], F32)
        sum_mean = sb("sum_mean", [P, CT], F32)
        gm = sb("gm", [P, CT], F32)
        dm = sb("dm", [P, CT, RUNS], F32)
        spread = sb("spread", [P, CT], F32)
        gv = sb("gv", [P, CT], F32)
        rs = [sb(f"rs{n}", [P, CT], F32) for n in range(4)]
        nt = sb("nt", [P, CT], F32)
        nu = sb("nu", [P, CT], F32)
        row_max = sb("row_max", [P, CT], F32)
        row_bias = sb("row_bias", [P, CT], F32)
        Z = sb("Z", [P, CT], F32)
        rz = sb("rz", [P, CT], F32)
        rz15 = sb("rz15", [P, CT], F32)

        runs = bn[:, :, :, :].rearrange("p t h (s k) -> p t (h s) k", k=3)
        run_mean, run_m2 = runs[:, :, :, 1], runs[:, :, :, 2]

        gram = [ctx.enter_context(nc.psum_tensor(f"gram{r}", [P, BANK], F32)) for r in range(CT)]
        acc = [ctx.enter_context(nc.psum_tensor(f"acc{r}", [P, BANK], F32)) for r in range(ACCS)]
        mix = gram[CT - 1]

        w_loaded = [sem(f"w_loaded{t}") for t in range(CT)]
        b_loaded = sem("b_loaded")
        x0_loaded = [sem(f"x0_loaded{t}") for t in range(CT)]
        x_loaded = [sem(f"x_loaded{u}") for u in range(2)]
        stored = [sem(f"stored{u}") for u in range(2)]
        last_stored = sem("last_stored")
        zeroed = sem("zeroed")
        consts_ready = sem("consts_ready")
        bounds_ready = sem("bounds_ready")
        bounds_spread = sem("bounds_spread")
        l1_ready = sem("l1_ready")
        setup_step = sem("setup_step")
        scales_ready = sem("scales_ready")
        w_turned = sem("w_turned")
        w_high = sem("w_high")
        w_low = sem("w_low")
        stats_step = sem("stats_step")
        means_ready = sem("means_ready")
        means_mixed = sem("means_mixed")
        mix_read = sem("mix_read")
        xn_ready = sem("xn_ready")
        xh_ready = sem("xh_ready")
        xl_ready = sem("xl_ready")
        y_summed = sem("y_summed")
        y32_ready = sem("y32_ready")
        yh_ready = sem("yh_ready")
        yl_ready = sem("yl_ready")
        turn_allowed = sem("turn_allowed")
        yT_ready = [sem(f"yT_ready{h}") for h in range(2)]
        row_summed = sem("row_summed")
        yTs_ready = sem("yTs_ready")
        upper_ready = sem("upper_ready")
        row_complete = sem("row_complete")
        row_mirrored = sem("row_mirrored")
        max_ready = sem("max_ready")
        row_bias_ready = sem("row_bias_ready")
        exp_ready = sem("exp_ready")
        recip_ready = sem("recip_ready")
        rz15_ready = sem("rz15_ready")
        ah_ready = sem("ah_ready")
        al_ready = sem("al_ready")
        out_summed = sem("out_summed")
        out_added = sem("out_added")

        NEWTON = 3
        STATS_STEPS = 2 * CT + 3 + 2 + 3 * NEWTON

        def need(eng, s, value):
            if not isinstance(value, int) or value > 0:
                eng.wait_ge(s, value)

        def x_slot(b, lo, size):
            if isinstance(b.pair, int):
                start = (b.index() % SLOTS) * CT * N + lo
                return x_sb[:, start:start + size]
            return x_sb[:, bass.ds((b.pair % 2) * (2 * CT * N) + (b.parity * CT * N + lo), size)]

        def loads(b):
            return b.pair * DMA + b.parity * DMA

        def batch_of(dram, b):
            if isinstance(b.pair, int):
                return dram[b.index()]
            return dram[bass.ds(b.index(), 1)].rearrange("b p t n -> (b p) t n")

        def steps(eng, step, first=None):
            if first:
                first(Batch(0, 0))
            else:
                step(Batch(-1, 0), False, False, True)
            step(Batch(-1, 1), False, True, True)
            step(Batch(0, 0), True, True, True)
            step(Batch(0, 1), True, True, True)
            with eng.Fori(1, B // 2 - 1) as pair:
                step(Batch(pair, 0), True, True, True)
                step(Batch(pair, 1), True, True, True)
            step(Batch(B // 2 - 1, 0), True, True, False)
            step(Batch(B // 2 - 1, 1), True, False, False)

        block = ctx.enter_context(nc.Block())

        @block.sync
        def _(sp):
            def load(b):
                sp.dma_start(x_slot(b, 0, CT * N).rearrange("p (t n) -> p t n", t=CT),
                             batch_of(x_d, b)).then_inc(x_loaded[b.parity], DMA)

            def store(b):
                for t in range(CT):
                    sp.wait_ge(out_added, b.count(UNITS, 2 * t + 2))
                    sp.dma_start(batch_of(out_d, b)[:, t, :],
                                 x_slot(b, t * N, N)).then_inc(stored[b.parity], DMA)

            def store_last(b):
                for u in range(UNITS):
                    t, h = u // 2, u % 2
                    sp.wait_ge(out_added, b.count(UNITS, u + 1))
                    sp.dma_start(batch_of(out_d, b)[:, t, h * HALF:(h + 1) * HALF],
                                 x_slot(b, t * N + h * HALF, HALF)).then_inc(last_stored, DMA)

            def turn_y(b, u):
                h, m = u // CT, u % CT
                if u == 0:
                    need(sp, row_summed, b.count(CT, 0))
                    sp.sem_inc(turn_allowed, 1)
                sp.wait_ge(yl_ready, b.count(UNITS, u + 1))
                sp.sem_inc(turn_allowed, 1)
                sp.dma_start_transpose(
                    yT[:, h, :, :, m * P:(m + 1) * P].rearrange("p a j c -> p (a j) c"),
                    y16[b.parity][:, h, m, :, :].rearrange("p a q -> p (a q)")).then_inc(yT_ready[h], DMA)

            def refill(b):
                sp.wait_ge(stored[b.parity], (b.pair + 1) * (CT * DMA))
                load(b.plus(SLOTS))

            for t in range(CT):
                sp.dma_start(w_sb[:, t, :], W[t * P:(t + 1) * P, :]).then_inc(w_loaded[t], DMA)
            first = Batch(0, 0)
            for t in range(CT):
                sp.dma_start(x_slot(first, t * N, N), batch_of(x_d, first)[:, t, :]).then_inc(x0_loaded[t], DMA)
            load(Batch(0, 1))
            load(Batch(1, 0))
            sp.wait_ge(x_loaded[1], DMA)
            load(Batch(1, 1))

            def step(b, do_gram, do_y, do_load):
                if do_y:
                    for u in range(UNITS):
                        turn_y(b.plus(1), u)
                if do_gram:
                    store(b)
                if do_load:
                    refill(b)

            step(Batch(-1, 1), False, True, False)
            step(Batch(0, 0), True, True, True)
            step(Batch(0, 1), True, True, True)
            with sp.Fori(1, (B - SLOTS) // 2) as pair:
                step(Batch(pair, 0), True, True, True)
                step(Batch(pair, 1), True, True, True)
            for n in range(B - SLOTS, B - 1):
                step(Batch(n // 2, n % 2), True, True, False)
            store_last(Batch(B // 2 - 1, 1))
            sp.wait_ge(stored[0], B // 2 * CT * DMA)
            sp.wait_ge(stored[1], (B // 2 - 1) * CT * DMA)
            sp.wait_ge(last_stored, UNITS * DMA)

        @block.gpsimd
        def _(pool):
            nc.gpsimd.memset(ident[:, :], 0.0).then_inc(zeroed, 1)
            nc.gpsimd.memset(gmean[:, :], 1.0 / GSIZE).then_inc(zeroed, 1)
            pool.wait_ge(zeroed, 2)
            nc.gpsimd.affine_select(out=ident[:, :], in_=ident[:, :], compare_op=ALU.not_equal, fill=1.0,
                                    base=0, pattern=[[-1, P]], channel_multiplier=1).then_inc(zeroed, 1)
            blocks = gmean[:, :].rearrange("p (g j) -> p g j", j=GSIZE)
            nc.gpsimd.affine_select(out=blocks, in_=blocks, compare_op=ALU.is_ge, fill=0.0, base=0,
                                    pattern=[[-GSIZE, P // GSIZE], [0, GSIZE]],
                                    channel_multiplier=1).then_inc(zeroed, 1)
            pool.wait_ge(zeroed, 4)
            nc.gpsimd.affine_select(out=blocks, in_=blocks, compare_op=ALU.is_ge, fill=0.0, base=GSIZE - 1,
                                    pattern=[[GSIZE, P // GSIZE], [0, GSIZE]],
                                    channel_multiplier=-1).then_inc(consts_ready, 1)
            pool.wait_ge(bounds_ready, 2)
            nc.gpsimd.partition_all_reduce(bounds_all[:, :], bounds[:, :], P,
                                           bass.bass_isa.ReduceOp.max).then_inc(bounds_spread, 1)

        @block.tensor
        def _(pe):
            pe.wait_ge(consts_ready, 1)
            for m in range(CT):
                pe.wait_ge(w_loaded[m], DMA)
                for k in range(CT):
                    mm = nc.tensor.transpose(acc[k][:, m * P:(m + 1) * P],
                                             w_sb[:, m, k * P:(k + 1) * P], ident[:, :])
            mm.then_inc(w_turned, 1)

            def gram_row(b, r, y_follows):
                if r == CT - 1 and y_follows:
                    pe.wait_ge(mix_read, b.plus(1).count(2, 2))
                need(pe, exp_ready, b.count(CT, 0))
                own, right = slice(r * P, (r + 1) * P), slice((r + 1) * P, C)
                last = r == CT - 1
                for j in range(NT):
                    h, jt = j // CT, j % CT
                    if r == 0 and jt == 0:
                        pe.wait_ge(yTs_ready, b.count(2, h + 1))
                    high, low = yT[:, h, 0, jt, :], yT[:, h, 1, jt, :]
                    mm = nc.tensor.matmul(gram[r][:, own], yTs[:, h, jt, own], high[:, own],
                                          start=(j == 0), stop=False)
                    if not last:
                        mm = nc.tensor.matmul(gram[r][:, right], high[:, own], high[:, right],
                                              start=False, stop=False)
                    mm = nc.tensor.matmul(gram[r][:, r * P:C], high[:, own], low[:, r * P:C],
                                          start=False, stop=(last and j == NT - 1))
                    if not last:
                        mm = nc.tensor.matmul(gram[r][:, right], low[:, own], high[:, right],
                                              start=False, stop=(j == NT - 1))
                mm.then_inc(row_summed, 1)

            def mirror_row(b, r):
                pe.wait_ge(upper_ready, b.count(CT, r + 1))
                for c in range(r + 1):
                    mm = nc.tensor.transpose(gram[r][:, c * P:(c + 1) * P],
                                             upper[:, c, r * P:(r + 1) * P], ident[:, :])
                mm.then_inc(row_mirrored, 1)

            def y_products(b, u, k):
                h, cols = u // CT, slice((u % CT) * P, (u % CT + 1) * P)
                if u == 0:
                    pe.wait_ge(xh_ready, b.count(CT, k + 1))
                    pe.wait_ge(xl_ready, b.count(CT, k + 1))
                for wt, xt in ((wTh, xh), (wTh, xl), (wTl, xh)):
                    mm = nc.tensor.matmul(acc[u % ACCS][:, :], wt[:, k, cols], xt[:, k, h, :],
                                          start=(k == 0 and wt is wTh and xt is xh),
                                          stop=(k == CT - 1 and wt is wTl))
                if k == CT - 1:
                    mm.then_inc(y_summed, 1)

            def y_unit(b, u):
                if u >= ACCS:
                    pe.wait_ge(yh_ready, b.count(UNITS, u - ACCS + 1))
                elif u == 0:
                    need(pe, out_added, b.plus(-1).count(UNITS, 0))
                for k in range(CT):
                    y_products(b, u, k)

            def first_y_units(b):
                pe.wait_ge(w_low, CT)
                for k in range(CT):
                    for u in range(ACCS):
                        y_products(b, u, k)

            def out_products(b, u, k):
                h, rows = u % 2, slice(u // 2 * P, (u // 2 + 1) * P)
                if u == 0:
                    pe.wait_ge(ah_ready, b.count(CT, k + 1))
                    pe.wait_ge(al_ready, b.count(CT, k + 1))
                for a, at in ((0, Ah), (0, Al), (1, Ah)):
                    mm = nc.tensor.matmul(acc[u % ACCS][:, :], y16[b.parity][:, h, k, a, rows], at[:, k, :],
                                          start=(k == 0 and a == 0 and at is Ah),
                                          stop=(k == CT - 1 and a == 1))
                if k == CT - 1:
                    mm.then_inc(out_summed, 1)

            def out_unit(b, u):
                if u >= ACCS:
                    pe.wait_ge(out_added, b.count(UNITS, u - ACCS + 1))
                else:
                    pe.wait_ge(yh_ready, b.plus(1).count(UNITS, UNITS - ACCS + u + 1))
                for k in range(CT):
                    out_products(b, u, k)

            def first_out_units_of_last(b):
                for k in range(CT):
                    for u in range(ACCS):
                        if k == 0:
                            pe.wait_ge(out_added, b.plus(-1).count(UNITS, UNITS - ACCS + u + 1))
                        out_products(b, u, k)

            def mix_means(b, k):
                pe.wait_ge(means_ready, b.count(2, k + 1))
                if k == 0:
                    need(pe, exp_ready, b.plus(-1).count(CT, 0))
                rhs = sum_mean[:, :] if k == 0 else spread[:, :]
                nc.tensor.matmul(mix[:, k * CT:(k + 1) * CT], gmean[:, :], rhs,
                                 start=True, stop=True).then_inc(means_mixed, 1)

            def step(b, do_gram, do_y, do_norm):
                nxt, norm = b.plus(1), b.plus(2)
                if do_gram:
                    gram_row(b, 0, do_y)
                    gram_row(b, 1, do_y)
                    mirror_row(b, 0)
                    gram_row(b, 2, do_y)
                    mirror_row(b, 1)
                    gram_row(b, 3, do_y)
                filling = not do_gram
                for u in range(UNITS):
                    if do_y:
                        if not filling or u >= ACCS:
                            y_unit(nxt, u)
                        elif u == 0:
                            first_y_units(nxt)
                    if u == 0 and do_gram:
                        mirror_row(b, 2)
                        mirror_row(b, 3)
                    if filling and do_norm and u in (5, 7):
                        mix_means(norm, u // 2 - 2)
                for u in range(UNITS):
                    if do_gram:
                        if do_y or u >= ACCS:
                            out_unit(b, u)
                        elif u == 0:
                            first_out_units_of_last(b)
                    if not filling and do_norm and u in (1, 4):
                        mix_means(norm, u // 4)

            steps(pe, step)

        @block.scalar
        def _(act):
            with nc.allow_non_contiguous_dma(reason="the bias, 4 bytes for each channel, once"):
                act.dma_start(b_sb[:, :], bias.rearrange("(t p) -> p t", p=P)).then_inc(b_loaded, DMA)
            for t in range(CT):
                act.wait_ge(w_loaded[t], DMA)
                nc.scalar.activation(E[:, t, :], w_sb[:, t, :], ACT.Abs,
                                     accum_out=w_l1[:, t:t + 1]).then_inc(l1_ready, 1)
            act.wait_ge(scales_ready, 1)
            act.wait_ge(w_turned, 1)
            for k in range(CT):
                nc.scalar.activation(wTh[:, k, :], acc[k][:, :], ACT.Copy, scale=scales[:, 0:1]).then_inc(w_high, 1)
            act.wait_ge(scales_ready, 2)

            def exp_row(b, r):
                act.wait_ge(row_bias_ready, b.count(CT, r + 1))
                need(act, al_ready, b.count(CT, 0))
                nc.scalar.activation(E[:, r, :], gram[r][:, :], ACT.Exp, bias=row_bias[:, r:r + 1],
                                     scale=kappa[:, 0:1], accum_out=Z[:, r:r + 1]).then_inc(exp_ready, 1)

            def prob_high(b, r):
                act.wait_ge(rz15_ready, b.count(CT, r + 1))
                need(act, out_summed, b.count(UNITS, 0))
                nc.scalar.activation(Ah[:, r, :], E[:, r, :], ACT.Copy,
                                     scale=rz15[:, r:r + 1]).then_inc(ah_ready, 1)

            def y_high(b, u):
                h, m = u // CT, u % CT
                act.wait_ge(y_summed, b.count(UNITS, u + 1))
                need(act, yl_ready, b.count(UNITS, u - 1))
                need(act, out_summed, b.plus(-1).count(UNITS, 0))
                nc.scalar.activation(y32[:, u % 2, :], acc[u % ACCS][:, :], ACT.Identity,
                                     bias=y_bias[:, m:m + 1], scale=y_scale[:, 0:1]).then_inc(y32_ready, 1)
                nc.scalar.activation(y16[b.parity][:, h, m, 0, :], acc[u % ACCS][:, :], ACT.Identity,
                                     bias=y_bias[:, m:m + 1], scale=y_scale[:, 0:1]).then_inc(yh_ready, 1)

            def x_high(b, t):
                act.wait_ge(xn_ready, b.count(CT, t + 1))
                need(act, y_summed, b.count(UNITS, 0))
                nc.scalar.activation(xh[:, t, :, :], xn[:, t % 2, :].rearrange("p (q h) -> p h q", h=2),
                                     ACT.Copy).then_inc(xh_ready, 1)

            def step(b, do_gram, do_y, do_norm):
                nxt, norm = b.plus(1), b.plus(2)
                if do_gram:
                    exp_row(b, 0)
                    exp_row(b, 1)
                    prob_high(b, 0)
                for u in range(UNITS):
                    if do_y:
                        y_high(nxt, u)
                    if do_gram:
                        if u == 0:
                            exp_row(b, 2)
                            prob_high(b, 1)
                            exp_row(b, 3)
                        if u in (1, 2):
                            prob_high(b, u + 1)
                if do_norm:
                    for t in range(CT):
                        x_high(norm, t)

            steps(act, step)

        @block.vector
        def _(dve):
            v = nc.vector

            count = [0]

            def chain(ins):
                count[0] += 1
                ins.then_inc(setup_step, 1)
                dve.wait_ge(setup_step, count[0])

            def find_bounds():
                dve.wait_ge(b_loaded, DMA)
                chain(v.tensor_reduce(b_abs[:, :], b_sb[:, :].rearrange("p (t o) -> p t o", o=1), AX.X, ALU.max,
                                      apply_absolute_value=True))
                dve.wait_ge(l1_ready, CT)
                chain(v.scalar_tensor_tensor(y_l1[:, :], w_l1[:, :], XN_BOUND, b_abs[:, :], ALU.mult, ALU.add))
                v.tensor_reduce(bounds[:, 0:1], w_l1[:, :], AX.X, ALU.max).then_inc(bounds_ready, 1)
                v.tensor_reduce(bounds[:, 1:2], y_l1[:, :], AX.X, ALU.max).then_inc(bounds_ready, 1)

            def find_scales():
                dve.wait_ge(bounds_spread, 1)
                chain(v.tensor_scalar(bounds_all[:, :], bounds_all[:, :], LEAST_BOUND, None, ALU.max))
                chain(v.tensor_scalar(pow2[:, :].bitcast(U32), bounds_all[:, :].bitcast(U32), EXPONENT_BITS, None,
                                      ALU.bitwise_and))
                chain(v.tensor_scalar(unscales[:, :], pow2[:, :], 1.0 / FP16_TOP, None, ALU.mult))
                v.reciprocal(scales[:, :], unscales[:, :]).then_inc(scales_ready, 1)
                v.tensor_scalar(out_scale[:, :], unscales[:, 1:2], 1.0 / PROB_SCALE, None, ALU.mult)
                chain(v.tensor_scalar(kappa[:, :], unscales[:, 1:2], unscales[:, 1:2], None, ALU.mult))
                v.tensor_scalar(neg_kappa[:, :], kappa[:, :], -1.0, None, ALU.mult)
                dve.wait_ge(scales_ready, 1)
                v.tensor_scalar(y_bias[:, :], b_sb[:, :], scales[:, 1:2], None, ALU.mult)
                v.tensor_scalar(y_scale[:, :], scales[:, 1:2], unscales[:, 0:1], 1.0 / XN_SCALE,
                                ALU.mult, ALU.mult).then_inc(scales_ready, 1)

            def w_low_half(k):
                dve.wait_ge(w_high, k + 1)
                v.scalar_tensor_tensor(wTl[:, k, :], acc[k][:, :], scales[:, 0:1], wTh[:, k, :],
                                       ALU.mult, ALU.subtract).then_inc(w_low, 1)

            def channel_stats(b, piece):
                t, h = piece // 2, piece % 2
                if isinstance(b.pair, int) and b.index() == 0:
                    dve.wait_ge(x0_loaded[t], DMA)
                elif piece == 0:
                    dve.wait_ge(x_loaded[b.parity], loads(b))
                v.bn_stats(bn[:, t, h, :], x_slot(b, t * N + h * HALF, HALF)).then_inc(stats_step, 1)

            def channel_means(b):
                dve.wait_ge(stats_step, b.count(STATS_STEPS, 2 * CT))
                v.tensor_reduce(sum_mean[:, :], run_mean, AX.X, ALU.add).then_inc(means_ready, 1)

            def group_mean(b):
                dve.wait_ge(means_mixed, b.count(2, 1))
                v.tensor_scalar(gm[:, :], mix[:, 0:CT], 1.0 / RUNS, None, ALU.mult).then_inc(mix_read, 1)
                dve.wait_ge(mix_read, b.count(2, 1))
                v.tensor_tensor(dm[:, :, :], run_mean, gm[:, :].unsqueeze(2).broadcast_to([P, CT, RUNS]),
                                ALU.subtract).then_inc(stats_step, 1)
                dve.wait_ge(stats_step, b.count(STATS_STEPS, 2 * CT + 1))
                v.tensor_tensor(dm[:, :, :], dm[:, :, :], dm[:, :, :], ALU.mult).then_inc(stats_step, 1)
                dve.wait_ge(stats_step, b.count(STATS_STEPS, 2 * CT + 2))
                v.scalar_tensor_tensor(dm[:, :, :], run_m2, RUNS / N, dm[:, :, :],
                                       ALU.mult, ALU.add).then_inc(stats_step, 1)
                dve.wait_ge(stats_step, b.count(STATS_STEPS, 2 * CT + 3))
                v.tensor_reduce(spread[:, :], dm[:, :, :], AX.X, ALU.add).then_inc(means_ready, 1)

            def group_rsqrt(b):
                k = 2 * CT + 3
                dve.wait_ge(means_mixed, b.count(2, 2))
                v.tensor_scalar(gv[:, :], mix[:, CT:2 * CT], RUNS * GN_EPS, XN_SCALE ** -2 / RUNS,
                                ALU.add, ALU.mult).then_inc(mix_read, 1)
                dve.wait_ge(mix_read, b.count(2, 2))
                v.tensor_scalar(nt[:, :].bitcast(I32), gv[:, :].bitcast(I32), 1, None,
                                ALU.arith_shift_right).then_inc(stats_step, 1)
                k += 1
                dve.wait_ge(stats_step, b.count(STATS_STEPS, k))
                v.tensor_scalar(rs[0][:, :].bitcast(I32), nt[:, :].bitcast(I32), -1.0, RSQRT_SEED,
                                ALU.mult, ALU.add).then_inc(stats_step, 1)
                k += 1
                for n in range(NEWTON):
                    dve.wait_ge(stats_step, b.count(STATS_STEPS, k))
                    v.scalar_tensor_tensor(nt[:, :], rs[n][:, :], -0.5, rs[n][:, :],
                                           ALU.mult, ALU.mult).then_inc(stats_step, 1)
                    dve.wait_ge(stats_step, b.count(STATS_STEPS, k + 1))
                    v.tensor_tensor(nu[:, :], nt[:, :], gv[:, :], ALU.mult).then_inc(stats_step, 1)
                    dve.wait_ge(stats_step, b.count(STATS_STEPS, k + 2))
                    v.scalar_tensor_tensor(rs[n + 1][:, :], nu[:, :], 1.5, rs[n][:, :],
                                           ALU.add, ALU.mult).then_inc(stats_step, 1)
                    k += 3
                assert k == STATS_STEPS

            def x_normalise(b, t):
                if t == 0:
                    dve.wait_ge(stats_step, b.count(STATS_STEPS, STATS_STEPS))
                need(dve, xh_ready, b.count(CT, t - 1))
                need(dve, xl_ready, b.count(CT, t - 1))
                v.tensor_scalar(xn[:, t % 2, :], x_slot(b, t * N, N), gm[:, t:t + 1],
                                rs[NEWTON][:, t:t + 1], ALU.subtract, ALU.mult).then_inc(xn_ready, 1)

            def x_low(b, t):
                dve.wait_ge(xh_ready, b.count(CT, t + 1))
                v.tensor_tensor(xl[:, t, :, :], xn[:, t % 2, :].rearrange("p (q h) -> p h q", h=2),
                                xh[:, t, :, :], ALU.subtract).then_inc(xl_ready, 1)

            def x_split_piece(b, piece):
                if piece == 0:
                    x_normalise(b, 0)
                    x_normalise(b, 1)
                elif piece < CT - 1:
                    x_low(b, piece - 1)
                    x_normalise(b, piece + 1)
                else:
                    x_low(b, CT - 2)
                    x_low(b, CT - 1)

            def halve_yT(b, h):
                dve.wait_ge(yT_ready[h], b.count(CT * DMA, CT * DMA))
                need(dve, row_summed, b.count(CT, 0))
                v.tensor_scalar(yTs[:, h, :, :], yT[:, h, 0, :, :], 0.5, None, ALU.mult).then_inc(yTs_ready, 1)

            def keep_upper(b, r):
                dve.wait_ge(row_summed, b.count(CT, r + 1))
                need(dve, row_mirrored, b.count(CT, 0))
                v.tensor_copy(upper[:, r, r * P:C], gram[r][:, r * P:C]).then_inc(upper_ready, 1)

            def row_maximum(b, r):
                own = slice(r * P, (r + 1) * P)
                dve.wait_ge(row_mirrored, b.count(CT, r + 1))
                v.tensor_tensor(gram[r][:, own], gram[r][:, own], upper[:, r, own],
                                ALU.add).then_inc(row_complete, 1)
                dve.wait_ge(row_complete, b.count(CT, r + 1))
                need(dve, exp_ready, b.count(CT, 0))
                v.tensor_reduce(row_max[:, r:r + 1], gram[r][:, :], AX.X, ALU.max).then_inc(max_ready, 1)
                dve.wait_ge(max_ready, b.count(CT, r + 1))
                v.tensor_scalar(row_bias[:, r:r + 1], row_max[:, r:r + 1], neg_kappa[:, 0:1], None,
                                ALU.mult).then_inc(row_bias_ready, 1)

            def row_reciprocal(b, r):
                dve.wait_ge(exp_ready, b.count(CT, r + 1))
                v.reciprocal(rz[:, r:r + 1], Z[:, r:r + 1]).then_inc(recip_ready, 1)
                dve.wait_ge(recip_ready, b.count(CT, r + 1))
                v.tensor_scalar(rz15[:, r:r + 1], rz[:, r:r + 1], PROB_SCALE, None,
                                ALU.mult).then_inc(rz15_ready, 1)

            def prob_low(b, r):
                dve.wait_ge(ah_ready, b.count(CT, r + 1))
                v.scalar_tensor_tensor(Al[:, r, :], E[:, r, :], rz15[:, r:r + 1], Ah[:, r, :],
                                       ALU.mult, ALU.subtract).then_inc(al_ready, 1)

            def y_low(b, u):
                h, m = u // CT, u % CT
                dve.wait_ge(yh_ready, b.count(UNITS, u + 1))
                v.tensor_tensor(y16[b.parity][:, h, m, 1, :], y32[:, u % 2, :], y16[b.parity][:, h, m, 0, :],
                                ALU.subtract).then_inc(yl_ready, 1)

            def add_out(b, u):
                t, h = u // 2, u % 2
                dve.wait_ge(out_summed, b.count(UNITS, u + 1))
                x_part = x_slot(b, t * N + h * HALF, HALF)
                v.scalar_tensor_tensor(x_part, acc[u % ACCS][:, :], out_scale[:, 0:1], x_part,
                                       ALU.mult, ALU.add).then_inc(out_added, 1)

            def step(b, do_gram, do_y, do_norm):
                nxt, norm = b.plus(1), b.plus(2)

                def stats(*pieces):
                    if do_norm:
                        for piece in pieces:
                            channel_stats(norm, piece)

                stats(0, 1)
                if do_gram:
                    keep_upper(b, 0)
                stats(2, 3)
                if do_gram:
                    keep_upper(b, 1)
                    row_maximum(b, 0)
                stats(4, 5)
                if do_gram:
                    keep_upper(b, 2)
                    row_maximum(b, 1)
                    row_reciprocal(b, 0)
                    keep_upper(b, 3)
                    prob_low(b, 0)
                stats(6, 7)
                if do_gram:
                    row_reciprocal(b, 1)
                    row_maximum(b, 2)
                    row_maximum(b, 3)
                    prob_low(b, 1)
                if do_norm:
                    channel_means(norm)
                for u in range(UNITS):
                    if do_gram and u in (1, 2):
                        row_reciprocal(b, u + 1)
                    if do_y:
                        y_low(nxt, u)
                    if do_gram and u in (2, 3):
                        prob_low(b, u)
                    if not do_gram and u == 5:
                        group_mean(norm)
                    if not do_gram and u == 6:
                        halve_yT(nxt, 0)
                if not do_gram:
                    group_rsqrt(norm)
                for u in range(UNITS):
                    if do_gram:
                        add_out(b, u)
                        if do_y and u in (1, 5):
                            halve_yT(nxt, u // 4)
                    if do_norm:
                        if u == 2 and do_gram:
                            group_mean(norm)
                        if u == 4 and do_gram:
                            group_rsqrt(norm)
                        if u >= 4:
                            x_split_piece(norm, u - 4)
                        if u == 4 and not do_gram:
                            halve_yT(nxt, 1)

            def first(b):
                find_bounds()
                channel_stats(b, 0)
                channel_stats(b, 1)
                find_scales()
                for piece in range(2, 2 * CT):
                    channel_stats(b, piece)
                channel_means(b)
                w_low_half(0)
                w_low_half(1)
                group_mean(b)
                w_low_half(2)
                w_low_half(3)
                group_rsqrt(b)
                for piece in range(4):
                    x_split_piece(b, piece)

            steps(dve, step, first)


_INS = ['x', 'L0_conv_W', 'L0_conv_bias']
_OUTS = [((32, 512, 32, 32), 'float32')]


def kernel(**inputs):
    import numpy as _np
    import concourse.bacc as _bacc
    from concourse import mybir as _mybir
    from concourse.bass_utils import run_bass_kernel_spmd as _run

    nc = _bacc.Bacc("TRN2", target_bir_lowering=False, num_devices=1)
    arrays, args = {}, []
    for name in _INS:
        a = _np.ascontiguousarray(inputs[name])
        arrays[f"in_{name}_dram"] = a
        args.append(nc.dram_tensor(f"in_{name}_dram", a.shape, _mybir.dt.from_np(a.dtype), kind="ExternalInput").ap())
    for i, (shape, dtype) in enumerate(_OUTS):
        dt = _mybir.dt.from_np(_np.dtype(dtype))
        args.append(nc.dram_tensor(f"out_{i}_dram", shape, dt, kind="ExternalOutput").ap())
    bass_groupnorm_pointwise_conv_channel_attention_residual_kernel(nc, *args)
    r = _run(nc, [arrays], core_ids=[0])
    got = tuple(r.results[0][f"out_{i}_dram"] for i in range(len(_OUTS)))
    return got[0]
```
